# Optimizing a Trainium2 kernel written in Bass

```python
import numpy as np
import jax
import jax.numpy as jnp

def _softmax(x, axis=-1):
    return jax.nn.softmax(x, axis=axis)

def _gelu(x):
    return jax.nn.gelu(x, approximate=True)

def _silu(x):
    return jax.nn.silu(x)

def _sigmoid(x):
    return jax.nn.sigmoid(x)

def _layernorm(x, axis=-1, eps=1e-05):
    m = jnp.mean(x, axis=axis, keepdims=True)
    v = jnp.var(x, axis=axis, keepdims=True)
    return (x - m) / jnp.sqrt(v + eps)

def _scatter_add(tgt, idx, src, axis=0):
    return tgt.at[idx].add(src)

def _segment_sum(src, seg, n):
    return jax.ops.segment_sum(src, seg, n)
kernel_name = 'mk_dlrm_tower_d1_rec_r8_e8f1c6'

def setup_inputs(seed: int=0):
    np.random.seed(seed)
    _w = jnp.asarray

    def _rec_inputs():
        import jax
        import jax.numpy as jnp
        _tk = jax.random.key(seed)
        dense_ctx = jax.random.normal(jax.random.fold_in(_tk, 190), (512, 16), jnp.float32)
        ids = jnp.stack([jax.random.randint(jax.random.fold_in(_tk, 200 + f), (512,), 0, v, jnp.int32) for f, v in enumerate([1000, 12500, 1250, 1250, 12500, 125000, 1250, 1250, 1250, 1000, 1000, 1250, 1250, 1000, 1000, 12500, 1250, 1250, 1250, 12500, 1000, 12500, 1000, 12500, 1000, 1000, 1250])], axis=1)
        tbl_0 = 0.05 * jax.random.normal(jax.random.fold_in(_tk, 500 + 0), (1000, 128), jnp.float32)
        tbl_1 = 0.05 * jax.random.normal(jax.random.fold_in(_tk, 500 + 1), (12500, 128), jnp.float32)
        tbl_2 = 0.05 * jax.random.normal(jax.random.fold_in(_tk, 500 + 2), (1250, 128), jnp.float32)
        tbl_3 = 0.05 * jax.random.normal(jax.random.fold_in(_tk, 500 + 3), (1250, 128), jnp.float32)
        tbl_4 = 0.05 * jax.random.normal(jax.random.fold_in(_tk, 500 + 4), (12500, 128), jnp.float32)
        tbl_5 = 0.05 * jax.random.normal(jax.random.fold_in(_tk, 500 + 5), (125000, 128), jnp.float32)
        tbl_6 = 0.05 * jax.random.normal(jax.random.fold_in(_tk, 500 + 6), (1250, 128), jnp.float32)
        tbl_7 = 0.05 * jax.random.normal(jax.random.fold_in(_tk, 500 + 7), (1250, 128), jnp.float32)
        tbl_8 = 0.05 * jax.random.normal(jax.random.fold_in(_tk, 500 + 8), (1250, 128), jnp.float32)
        tbl_9 = 0.05 * jax.random.normal(jax.random.fold_in(_tk, 500 + 9), (1000, 128), jnp.float32)
        tbl_10 = 0.05 * jax.random.normal(jax.random.fold_in(_tk, 500 + 10), (1000, 128), jnp.float32)
        tbl_11 = 0.05 * jax.random.normal(jax.random.fold_in(_tk, 500 + 11), (1250, 128), jnp.float32)
        tbl_12 = 0.05 * jax.random.normal(jax.random.fold_in(_tk, 500 + 12), (1250, 128), jnp.float32)
        tbl_13 = 0.05 * jax.random.normal(jax.random.fold_in(_tk, 500 + 13), (1000, 128), jnp.float32)
        tbl_14 = 0.05 * jax.random.normal(jax.random.fold_in(_tk, 500 + 14), (1000, 128), jnp.float32)
        tbl_15 = 0.05 * jax.random.normal(jax.random.fold_in(_tk, 500 + 15), (12500, 128), jnp.float32)
        tbl_16 = 0.05 * jax.random.normal(jax.random.fold_in(_tk, 500 + 16), (1250, 128), jnp.float32)
        tbl_17 = 0.05 * jax.random.normal(jax.random.fold_in(_tk, 500 + 17), (1250, 128), jnp.float32)
        tbl_18 = 0.05 * jax.random.normal(jax.random.fold_in(_tk, 500 + 18), (1250, 128), jnp.float32)
        tbl_19 = 0.05 * jax.random.normal(jax.random.fold_in(_tk, 500 + 19), (12500, 128), jnp.float32)
        tbl_20 = 0.05 * jax.random.normal(jax.random.fold_in(_tk, 500 + 20), (1000, 128), jnp.float32)
        tbl_21 = 0.05 * jax.random.normal(jax.random.fold_in(_tk, 500 + 21), (12500, 128), jnp.float32)
        tbl_22 = 0.05 * jax.random.normal(jax.random.fold_in(_tk, 500 + 22), (1000, 128), jnp.float32)
        tbl_23 = 0.05 * jax.random.normal(jax.random.fold_in(_tk, 500 + 23), (12500, 128), jnp.float32)
        tbl_24 = 0.05 * jax.random.normal(jax.random.fold_in(_tk, 500 + 24), (1000, 128), jnp.float32)
        tbl_25 = 0.05 * jax.random.normal(jax.random.fold_in(_tk, 500 + 25), (1000, 128), jnp.float32)
        tbl_26 = 0.05 * jax.random.normal(jax.random.fold_in(_tk, 500 + 26), (1250, 128), jnp.float32)
        _rk = jax.random.fold_in(_tk, 7)
        W_top1 = 0.0521996 * jax.random.normal(jax.random.fold_in(_tk, 801), (367, 512), jnp.float32)
        W_top2 = 0.0441942 * jax.random.normal(jax.random.fold_in(_tk, 802), (512, 256), jnp.float32)
        W_top3 = 0.0625 * jax.random.normal(jax.random.fold_in(_tk, 803), (256, 1), jnp.float32)
        b_top1 = jnp.zeros((512,), jnp.float32)
        b_top2 = jnp.zeros((256,), jnp.float32)
        return (dense_ctx, ids, tbl_0, tbl_1, tbl_2, tbl_3, tbl_4, tbl_5, tbl_6, tbl_7, tbl_8, tbl_9, tbl_10, tbl_11, tbl_12, tbl_13, tbl_14, tbl_15, tbl_16, tbl_17, tbl_18, tbl_19, tbl_20, tbl_21, tbl_22, tbl_23, tbl_24, tbl_25, tbl_26, W_top1, b_top1, W_top2, b_top2, W_top3)
    dense_ctx, ids, tbl_0, tbl_1, tbl_2, tbl_3, tbl_4, tbl_5, tbl_6, tbl_7, tbl_8, tbl_9, tbl_10, tbl_11, tbl_12, tbl_13, tbl_14, tbl_15, tbl_16, tbl_17, tbl_18, tbl_19, tbl_20, tbl_21, tbl_22, tbl_23, tbl_24, tbl_25, tbl_26, W_top1, b_top1, W_top2, b_top2, W_top3 = _rec_inputs()

    def _L0_rec_setup():
        import jax, jax.numpy as jnp
        import numpy as np

        def _tri_indices(num_feas):
            return np.array([i * num_feas + j for j in range(1, num_feas) for i in range(j)], dtype=np.int32)
        key = jax.random.key(seed)
        batch, num_feas, embed_dim = (2048, 27, 128)
        inputs = jax.random.normal(key, (batch, num_feas, embed_dim), dtype=jnp.float32)
        return {'inputs': inputs, 'num_feas': num_feas}
    _L0_rec_all = _L0_rec_setup()
    _L0_rec_in = {k: v for k, v in _L0_rec_all.items() if k in ()}
    del _L0_rec_all
    return {'dense_ctx': dense_ctx, 'ids': ids, 'tbl_0': tbl_0, 'tbl_1': tbl_1, 'tbl_2': tbl_2, 'tbl_3': tbl_3, 'tbl_4': tbl_4, 'tbl_5': tbl_5, 'tbl_6': tbl_6, 'tbl_7': tbl_7, 'tbl_8': tbl_8, 'tbl_9': tbl_9, 'tbl_10': tbl_10, 'tbl_11': tbl_11, 'tbl_12': tbl_12, 'tbl_13': tbl_13, 'tbl_14': tbl_14, 'tbl_15': tbl_15, 'tbl_16': tbl_16, 'tbl_17': tbl_17, 'tbl_18': tbl_18, 'tbl_19': tbl_19, 'tbl_20': tbl_20, 'tbl_21': tbl_21, 'tbl_22': tbl_22, 'tbl_23': tbl_23, 'tbl_24': tbl_24, 'tbl_25': tbl_25, 'tbl_26': tbl_26, 'W_top1': W_top1, 'b_top1': b_top1, 'W_top2': W_top2, 'b_top2': b_top2, 'W_top3': W_top3}

def reference(dense_ctx, ids, tbl_0, tbl_1, tbl_2, tbl_3, tbl_4, tbl_5, tbl_6, tbl_7, tbl_8, tbl_9, tbl_10, tbl_11, tbl_12, tbl_13, tbl_14, tbl_15, tbl_16, tbl_17, tbl_18, tbl_19, tbl_20, tbl_21, tbl_22, tbl_23, tbl_24, tbl_25, tbl_26, W_top1, b_top1, W_top2, b_top2, W_top3):
    import jax
    import jax.numpy as jnp

    def _L0_rec_ref(inputs, num_feas):
        import jax, jax.numpy as jnp
        import numpy as np

        def _tri_indices(num_feas):
            return np.array([i * num_feas + j for j in range(1, num_feas) for i in range(j)], dtype=np.int32)
        dot = jnp.einsum('bnd,bmd->bnm', inputs, inputs)
        idx = jnp.asarray(_tri_indices(num_feas))
        flat = dot.reshape(inputs.shape[0], num_feas * num_feas)
        return flat[:, idx]
    e = jnp.stack([tbl_0[ids[:, 0]], tbl_1[ids[:, 1]], tbl_2[ids[:, 2]], tbl_3[ids[:, 3]], tbl_4[ids[:, 4]], tbl_5[ids[:, 5]], tbl_6[ids[:, 6]], tbl_7[ids[:, 7]], tbl_8[ids[:, 8]], tbl_9[ids[:, 9]], tbl_10[ids[:, 10]], tbl_11[ids[:, 11]], tbl_12[ids[:, 12]], tbl_13[ids[:, 13]], tbl_14[ids[:, 14]], tbl_15[ids[:, 15]], tbl_16[ids[:, 16]], tbl_17[ids[:, 17]], tbl_18[ids[:, 18]], tbl_19[ids[:, 19]], tbl_20[ids[:, 20]], tbl_21[ids[:, 21]], tbl_22[ids[:, 22]], tbl_23[ids[:, 23]], tbl_24[ids[:, 24]], tbl_25[ids[:, 25]], tbl_26[ids[:, 26]]], axis=1)
    z = _L0_rec_ref(e, 27)
    z = z.reshape(z.shape[0], -1)
    h = jnp.concatenate([z, dense_ctx], axis=1)
    h = jnp.maximum(h @ W_top1 + b_top1, 0.0)
    h = jnp.maximum(h @ W_top2 + b_top2, 0.0)
    y = h @ W_top3
    return y

_drawn_inputs = setup_inputs


def setup_inputs(seed=0):
    import zlib

    import numpy as np

    out = dict(_drawn_inputs(seed))
    spreads = {'b_top1': (0.0, 0.1), 'b_top2': (0.0, 0.1)}
    factors = {}
    for name, (base, spread) in spreads.items():
        noise = np.random.default_rng([zlib.crc32(name.encode()), seed]).standard_normal(out[name].shape)
        drawn = base * np.exp(spread * noise) if base else spread * noise
        out[name] = jnp.asarray(drawn.astype(out[name].dtype))
    for name, factor in factors.items():
        out[name] = (out[name] * factor).astype(out[name].dtype)
    return out
```

```python
from contextlib import ExitStack

import concourse.bass as bass
from concourse import mybir

F32 = mybir.dt.float32
F32R = mybir.dt.float32r
I32 = mybir.dt.int32
I16 = mybir.dt.int16
ALU = mybir.AluOpType
ACT = mybir.ActivationFunctionType

P = 128
BATCH = 512
DIM = 128
FEATURES = 27
DENSE = 16
HIDDEN1 = 512
HIDDEN2 = 256
TILES = BATCH // P
QUAD = 4
QUADS = P // QUAD

ROWS = [1000, 12500, 1250, 1250, 12500, 125000, 1250, 1250, 1250, 1000, 1000, 1250, 1250, 1000, 1000, 12500,
        1250, 1250, 1250, 12500, 1000, 12500, 1000, 12500, 1000, 1000, 1250]
PICK_ROWS = 1000
GATHER_FEATURES = [f for f in range(FEATURES) if ROWS[f] != PICK_ROWS]
PICK_FEATURES = [f for f in range(FEATURES) if ROWS[f] == PICK_ROWS]
SLOT_FEATURE = GATHER_FEATURES + PICK_FEATURES
GATHERED = len(GATHER_FEATURES)
PICKED = len(PICK_FEATURES)

TURN = 4
TURN_SLOTS = [range(a, min(a + TURN, GATHERED)) for a in range(0, GATHERED, TURN)]
TURNS = len(TURN_SLOTS)

CHUNKS = 8
PICK_PART = PICK_ROWS // CHUNKS
SPRAY = PICK_PART // 16 * 16
GROUP = 2
VECS = 3
HOT_SLOTS = 2 * CHUNKS

STEPS = (FEATURES - 1) // 2
WIDE = FEATURES + STEPS
GRAM_QUADS = 8
GRAMS = QUADS // GRAM_QUADS
PAIR_N = 9
PAIR_CHUNKS = FEATURES // PAIR_N
PAIR_PART = PAIR_N * STEPS
DENSE_FIRST = P - PAIR_PART
K_ROWS = [P, PAIR_PART + DENSE - DENSE_FIRST, PAIR_PART]
OUT1 = HIDDEN1 // P
OUT2 = HIDDEN2 // P


def plan():
    order = [("ids", i, 0) for i in range(PICKED)]

    def onehot(g, i):
        return [("onehot", g, i)]

    def turn(t, g):
        return [("turn", t, g)]

    def gram(t, j):
        return [("gram", t, j)]

    def mlp(t):
        return [("layer1", t, 0), ("layer2", t, 0), ("layer3", t, 0)]

    for i in range(PICKED):
        order += onehot(0, i)
        if 1 <= i < 1 + TURNS:
            order += turn(0, i - 1)
    for j in range(GRAMS):
        order += gram(0, j)
    for j in range(4):
        order += onehot(1, j)
    for g in range(TURNS):
        order += turn(1, g)
    order += onehot(1, 4) + gram(1, 0) + onehot(1, 5) + gram(1, 1) + onehot(1, 6) + mlp(0)
    order += gram(1, 2) + onehot(1, 7) + gram(1, 3) + onehot(1, 8)
    for g in range(TURNS):
        order += turn(2, g)
    order += mlp(1)
    for j in range(GRAMS):
        order += gram(2, j)
    for g in range(TURNS - 1):
        order += turn(3, g)
    order += mlp(2)
    order += turn(3, TURNS - 1)
    for j in range(GRAMS):
        order += gram(3, j)
    order += mlp(3)
    return order


def build(nc, ids, dense, tables, w1, b1, w2, b2, w3, out):
    order = plan()
    turn_use = {s: n for n, s in enumerate(s for s in order if s[0] in ("ids", "turn"))}
    acc_use = {s: n for n, s in enumerate(s for s in order if s[0] in ("onehot", "layer1", "layer2", "layer3"))}
    gram_use = {s: n for n, s in enumerate(s for s in order if s[0] == "gram")}
    picks = [s for s in order if s[0] == "onehot"]

    with ExitStack() as ctx:
        def sb(name, shape, dt=F32):
            return ctx.enter_context(nc.sbuf_tensor(name, shape, dt))

        def ps(name, shape):
            return ctx.enter_context(nc.psum_tensor(name, shape, F32))

        def sem(name):
            return ctx.enter_context(nc.semaphore(name))

        ids_sb = sb("ids_sb", [P, TILES * FEATURES], I32)
        ids_f = sb("ids_f", [P, TILES * FEATURES])
        identity = sb("identity", [P, P])
        row_number_i = sb("row_number_i", [P, CHUNKS], I32)
        row_number = sb("row_number", [P, CHUNKS])
        ids_rows = sb("ids_rows", [P, PICKED, TILES * P], I16)
        raw = sb("raw", [P, GATHERED, DIM])
        table = sb("table", [PICK_PART, 2, CHUNKS * DIM])
        table_hi = sb("table_hi", [PICK_PART, PICKED, CHUNKS * DIM], F32R)
        table_lo = sb("table_lo", [PICK_PART, PICKED, CHUNKS * DIM], F32R)
        hot = sb("hot", [PICK_PART, HOT_SLOTS, GROUP * P], F32R)
        vec = sb("vec", [DIM, VECS, P, 32])
        dots = sb("dots", [32, FEATURES, QUAD, QUADS])
        pairs = sb("pairs", [P, PAIR_CHUNKS, BATCH])
        w1_sb = sb("w1_sb", [P, PAIR_CHUNKS, HIDDEN1])
        w2_sb = sb("w2_sb", [P, OUT1, HIDDEN2])
        w3_sb = sb("w3_sb", [P, OUT2])
        b1_sb = sb("b1_sb", [P, OUT1])
        b2_sb = sb("b2_sb", [P, OUT2])
        h1 = sb("h1", [P, OUT1, P])
        h2 = sb("h2", [P, OUT2, P])
        y = sb("y", [1, BATCH])

        turn_ps = ps("turn_ps", [P, 2, TURN, P])
        acc_ps = ps("acc_ps", [P, 2, 512])
        gram_ps = ps("gram_ps", [P, 2, GRAM_QUADS, P])

        scratch = nc.dram_tensor("scratch", [TILES, FEATURES, WIDE * P], F32, kind="Internal").ap()

        ids_in = sem("ids_in")
        table_in = [sem(f"table_in{r}") for r in range(2)]
        weights_in = sem("weights_in")
        dense_in = sem("dense_in")
        rows_in = [sem(f"rows_in{g}") for g in range(TURNS)]
        dots_out = sem("dots_out")
        pairs_in = [sem(f"pairs_in{t}") for t in range(TILES)]
        y_out = sem("y_out")
        zeroed = sem("zeroed")
        identity_made = sem("identity_made")
        rows_numbered = sem("rows_numbered")
        ids_float = sem("ids_float")
        numbers_float = sem("numbers_float")
        padded = sem("padded")
        hi_made = sem("hi_made")
        lo_made = sem("lo_made")
        hot_made = sem("hot_made")
        hot_used = sem("hot_used")
        turned = sem("turned")
        turn_read = sem("turn_read")
        acc_done = sem("acc_done")
        acc_read = sem("acc_read")
        gram_done = sem("gram_done")
        gram_read_act = sem("gram_read_act")
        gram_read_dve = sem("gram_read_dve")

        block = ctx.enter_context(nc.Block())

        def gram_read(s, use):
            return gram_ps[32 * s:32 * s + 32, use % 2, :, s * FEATURES:(s + 1) * FEATURES].rearrange("n q m -> n m q")

        def dots_at(s, j):
            return dots[:, :, s, j * GRAM_QUADS:(j + 1) * GRAM_QUADS]

        @block.sync
        def _(sp):
            def load_table(i):
                if i >= 2:
                    sp.wait_ge(lo_made, i - 1)
                src = tables[PICK_FEATURES[i]].rearrange("(p c) d -> p (c d)", c=CHUNKS)
                for a, b in ((0, SPRAY), (SPRAY, PICK_PART)):
                    sp.dma_start(table[a:b, i % 2, :], src[a:b, :]).then_inc(table_in[i % 2], 16)

            sp.dma_start(ids_sb[:, :], ids.rearrange("(p t) f -> p (t f)", t=TILES)).then_inc(ids_in, 16)
            for i in range(4):
                load_table(i)
            row = 0
            for c, k in enumerate(K_ROWS):
                sp.dma_start(w1_sb[0:k, c, :], w1[row:row + k, :]).then_inc(weights_in, 16)
                row += k
            sp.dma_start(w2_sb[:, :, :], w2.rearrange("(c p) n -> p c n", p=P)).then_inc(weights_in, 16)
            sp.dma_start(w3_sb[:, :], w3).then_inc(weights_in, 16)
            sp.dma_start(b1_sb[:, :], b1).then_inc(weights_in, 16)
            sp.dma_start(b2_sb[:, :], b2).then_inc(weights_in, 16)
            sp.dma_start(pairs[PAIR_PART:P, 0, :], dense[0:DENSE_FIRST, :]).then_inc(dense_in, 16)
            sp.dma_start(pairs[PAIR_PART:K_ROWS[1], 1, :], dense[DENSE_FIRST:DENSE, :]).then_inc(dense_in, 16)
            for i in range(4, PICKED):
                load_table(i)

            for t in range(TILES):
                sp.wait_ge(gram_read_act, GRAMS * (t + 1))
                sp.wait_ge(gram_read_dve, GRAMS * (t + 1))
                here = dots[0:FEATURES, :, :, :].rearrange("n m s q -> n (m s q)")
                sp.dma_start(scratch[t, :, 0:FEATURES * P], here).then_inc(dots_out, 16)
                sp.dma_start(scratch[t, :, FEATURES * P:], here[:, 0:STEPS * P]).then_inc(dots_out, 16)
                sp.wait_ge(dots_out, 32 * (t + 1))
                row_len = WIDE * P
                for c in range(PAIR_CHUNKS):
                    first = scratch[t, :, :]
                    n0 = c * PAIR_N
                    src = bass.AP(first.tensor, first.offset + n0 * row_len + (n0 + 1) * P,
                                  [[row_len + P, PAIR_N], [P, STEPS], [1, P]])
                    sp.dma_start(pairs[0:PAIR_PART, c, t * P:(t + 1) * P], src).then_inc(pairs_in[t], 16)

            sp.wait_ge(acc_read, acc_use["layer3", TILES - 1, 0] + 1)
            sp.dma_start(out.rearrange("b o -> o b"), y[:, :]).then_inc(y_out, 16)
            sp.wait_ge(y_out, 16)

        @block.gpsimd
        def _(pool):
            pool.memset(identity[:, :], 0.0).then_inc(zeroed, 1)
            pool.iota(row_number_i[:, :], pattern=[[1, CHUNKS]], base=0, channel_multiplier=CHUNKS)\
                .then_inc(rows_numbered, 1)
            pool.wait_ge(zeroed, 1)
            pool.affine_select(out=identity[:, :], in_=identity[:, :], compare_op=ALU.not_equal, fill=1.0,
                               base=0, pattern=[[-1, P]], channel_multiplier=1).then_inc(identity_made, 1)
            pool.wait_ge(ids_in, 16)
            for t in range(TILES):
                for g, slots in enumerate(TURN_SLOTS):
                    if t >= 1:
                        pool.wait_ge(turned, turn_use["turn", t - 1, g] + 1)
                    for n in slots:
                        f = SLOT_FEATURE[n]
                        at = t * FEATURES + f
                        pool.indirect_dma_start(raw[:, n, :], None, tables[f],
                                                bass.IndirectOffsetOnAxis(ap=ids_sb[:, at:at + 1], axis=0))\
                            .then_inc(rows_in[g], 16)

        @block.tensor
        def _(pe):
            for step in order:
                kind, t, g = step
                if kind in ("ids", "turn"):
                    use = turn_use[step]
                    bank = turn_ps[:, use % 2, :, :]
                    if use >= 2:
                        pe.wait_ge(turn_read, use - 1)
                    if kind == "ids":
                        if use == 0:
                            pe.wait_ge(identity_made, 1)
                            pe.wait_ge(ids_float, 1)
                        for tile in range(TILES):
                            at = tile * FEATURES + PICK_FEATURES[t]
                            last = pe.transpose(bank[:, tile, :], ids_f[:, at:at + 1].broadcast_to([P, P]),
                                                identity[:, :])
                    else:
                        slots = TURN_SLOTS[g]
                        pe.wait_ge(rows_in[g], 16 * len(slots) * (t + 1))
                        for x, n in enumerate(slots):
                            last = pe.transpose(bank[:, x, :], raw[:, n, :], identity[:, :])
                    last.then_inc(turned, 1)
                    continue
                if kind == "gram":
                    use = gram_use[step]
                    if g == 0:
                        pe.wait_ge(turn_read, turn_use["turn", t, TURNS - 1] + 1)
                        pe.wait_ge(acc_read, acc_use["onehot", t // GROUP, PICKED - 1] + 1)
                        if t == 0:
                            pe.wait_ge(padded, 1)
                    if use >= 2:
                        pe.wait_ge(gram_read_act, use - 1)
                        pe.wait_ge(gram_read_dve, use - 1)
                    for x in range(GRAM_QUADS):
                        q = g * GRAM_QUADS + x
                        quad = vec[:, t % VECS, q * QUAD:(q + 1) * QUAD, :]
                        last = pe.matmul(gram_ps[:, use % 2, x, 0:QUAD * FEATURES],
                                         quad.rearrange("d s f -> d (s f)"), quad[:, :, 0:FEATURES],
                                         start=True, stop=True)
                    last.then_inc(gram_done, 1)
                    continue
                use = acc_use[step]
                bank = acc_ps[:, use % 2, :]
                if use >= 2:
                    pe.wait_ge(acc_read, use - 1)
                if kind == "onehot":
                    group, i = t, g
                    pe.wait_ge(hi_made, i + 1)
                    pe.wait_ge(lo_made, i + 1)
                    for c in range(CHUNKS):
                        n = picks.index(step) * CHUNKS + c
                        pe.wait_ge(hot_made, n + 1)
                        rows = hot[:, n % HOT_SLOTS, :]
                        pe.matmul(bank[:, 0:GROUP * P], table_hi[:, i, c * DIM:(c + 1) * DIM], rows,
                                  start=(c == 0), stop=False)
                        last = pe.matmul(bank[:, 0:GROUP * P], table_lo[:, i, c * DIM:(c + 1) * DIM], rows,
                                         start=False, stop=(c == CHUNKS - 1))
                        if c < CHUNKS - 1:
                            last.then_inc(hot_used, 1)
                        else:
                            last.then_inc(acc_done, 1)
                elif kind == "layer1":
                    if t == 0:
                        pe.wait_ge(weights_in, 7 * 16)
                        pe.wait_ge(dense_in, 2 * 16)
                    pe.wait_ge(pairs_in[t], PAIR_CHUNKS * 16)
                    for o in range(OUT1):
                        for c, k in enumerate(K_ROWS):
                            last = pe.matmul(bank[:, o * P:(o + 1) * P], w1_sb[0:k, c, o * P:(o + 1) * P],
                                             pairs[0:k, c, t * P:(t + 1) * P],
                                             start=(c == 0), stop=(c == PAIR_CHUNKS - 1))
                    last.then_inc(acc_done, 1)
                elif kind == "layer2":
                    pe.wait_ge(acc_read, acc_use["layer1", t, 0] + 1)
                    for o in range(OUT2):
                        for c in range(OUT1):
                            last = pe.matmul(bank[:, o * P:(o + 1) * P], w2_sb[:, c, o * P:(o + 1) * P],
                                             h1[:, c, :], start=(c == 0), stop=(c == OUT1 - 1))
                    last.then_inc(acc_done, 1)
                else:
                    pe.wait_ge(acc_read, acc_use["layer2", t, 0] + 1)
                    for c in range(OUT2):
                        last = pe.matmul(bank[0:1, 0:P], w3_sb[:, c:c + 1], h2[:, c, :],
                                         start=(c == 0), stop=(c == OUT2 - 1))
                    last.then_inc(acc_done, 1)

        @block.scalar
        def _(act):
            def split_hi(i):
                act.wait_ge(table_in[i % 2], 32 * (i // 2 + 1))
                act.copy(table_hi[:, i, :], table[:, i % 2, :]).then_inc(hi_made, 1)

            split_hi(0)
            split_hi(1)
            for step in order:
                kind, t, g = step
                if kind == "ids":
                    use = turn_use[step]
                    act.wait_ge(turned, use + 1)
                    act.copy(ids_rows[:, t, :], turn_ps[:, use % 2, :, :].rearrange("p t b -> p (t b)"))\
                       .then_inc(turn_read, 1)
                elif kind == "turn":
                    use = turn_use[step]
                    slots = TURN_SLOTS[g]
                    act.wait_ge(turned, use + 1)
                    act.copy(vec[:, t % VECS, :, slots.start:slots.stop], turn_ps[:, use % 2, 0:len(slots), :].rearrange("d f p -> d p f"))\
                       .then_inc(turn_read, 1)
                elif kind == "onehot":
                    group, i = t, g
                    if group == 0 and i + 2 < PICKED:
                        split_hi(i + 2)
                    use = acc_use[step]
                    n = GATHERED + i
                    act.wait_ge(acc_done, use + 1)
                    for x in range(GROUP):
                        last = act.copy(vec[:, (group * GROUP + x) % VECS, :, n],
                                        acc_ps[:, use % 2, x * P:(x + 1) * P])
                    last.then_inc(acc_read, 1)
                elif kind == "gram":
                    use = gram_use[step]
                    if g == 0 and t >= 1:
                        act.wait_ge(dots_out, 32 * t)
                    act.wait_ge(gram_done, use + 1)
                    for s in (0, 1):
                        last = act.copy(dots_at(s, g), gram_read(s, use))
                    last.then_inc(gram_read_act, 1)
                elif kind == "layer1":
                    use = acc_use[step]
                    if t == 0:
                        act.wait_ge(weights_in, 7 * 16)
                    act.wait_ge(acc_done, use + 1)
                    for o in range(OUT1):
                        last = act.activation(h1[:, o, :], acc_ps[:, use % 2, o * P:(o + 1) * P], ACT.Relu,
                                              bias=b1_sb[:, o:o + 1])
                    last.then_inc(acc_read, 1)
                elif kind == "layer2":
                    use = acc_use[step]
                    act.wait_ge(acc_done, use + 1)
                    for o in range(OUT2):
                        last = act.activation(h2[:, o, :], acc_ps[:, use % 2, o * P:(o + 1) * P], ACT.Relu,
                                              bias=b2_sb[:, o:o + 1])
                    last.then_inc(acc_read, 1)
                else:
                    use = acc_use[step]
                    act.wait_ge(acc_done, use + 1)
                    dst = y[:, :].rearrange("o (q s t) -> o s q t", s=QUAD, t=TILES)[:, :, :, t]
                    act.copy(dst, acc_ps[0:1, use % 2, 0:P].rearrange("o (s q) -> o s q", s=QUAD))\
                       .then_inc(acc_read, 1)

        @block.vector
        def _(dve):
            def make_hot(k):
                _, group, i = picks[k]
                if group == 0:
                    dve.wait_ge(table_in[i % 2], 32 * (i // 2 + 1))
                    dve.wait_ge(hi_made, i + 1)
                    dve.tensor_tensor(table_lo[:, i, :], table[:, i % 2, :], table_hi[:, i, :].bitcast(F32),
                                      ALU.subtract).then_inc(lo_made, 1)
                    dve.wait_ge(turn_read, turn_use["ids", i, 0] + 1)
                for c in range(CHUNKS):
                    if k >= 2:
                        if c < CHUNKS - 1:
                            dve.wait_ge(hot_used, (k - 2) * (CHUNKS - 1) + c + 1)
                        else:
                            dve.wait_ge(acc_done, acc_use[picks[k - 2]] + 1)
                    n = k * CHUNKS + c
                    dve.tensor_scalar(hot[:, n % HOT_SLOTS, :],
                                      ids_rows[0:PICK_PART, i, group * GROUP * P:(group + 1) * GROUP * P],
                                      row_number[0:PICK_PART, c:c + 1], None, ALU.is_equal).then_inc(hot_made, 1)

            dve.memset(vec[:, :, :, FEATURES:], 0.0).then_inc(padded, 1)
            dve.wait_ge(rows_numbered, 1)
            dve.tensor_copy(row_number[:, :], row_number_i[:, :]).then_inc(numbers_float, 1)
            dve.wait_ge(ids_in, 16)
            dve.tensor_copy(ids_f[:, :], ids_sb[:, :]).then_inc(ids_float, 1)
            dve.wait_ge(numbers_float, 1)
            make_hot(0)
            for step in order:
                kind, t, g = step
                if kind == "onehot":
                    k = picks.index(step) + 1
                    if k < len(picks):
                        make_hot(k)
                elif kind == "gram":
                    use = gram_use[step]
                    if g == 0 and t >= 1:
                        dve.wait_ge(dots_out, 32 * t)
                    dve.wait_ge(gram_done, use + 1)
                    for s in (2, 3):
                        last = dve.tensor_copy(dots_at(s, g), gram_read(s, use))
                    last.then_inc(gram_read_dve, 1)


def pair_rows():
    dense_row = FEATURES * (FEATURES - 1) // 2
    rows = []
    for c in range(PAIR_CHUNKS):
        for n in range(c * PAIR_N, (c + 1) * PAIR_N):
            for k in range(1, STEPS + 1):
                i, j = sorted((SLOT_FEATURE[n], SLOT_FEATURE[(n + k) % FEATURES]))
                rows.append(j * (j - 1) // 2 + i)
        extra = K_ROWS[c] - PAIR_PART
        rows += range(dense_row, dense_row + extra)
        dense_row += extra
    return rows


def kernel(**inputs):
    import numpy as np
    import concourse.bacc as bacc
    from concourse.bass_utils import run_bass_kernel_spmd

    arrays = {"ids": inputs["ids"]}
    for f in range(FEATURES):
        arrays[f"tbl_{f}"] = inputs[f"tbl_{f}"]
    arrays["dense"] = np.asarray(inputs["dense_ctx"]).reshape(QUADS, QUAD, TILES, DENSE).transpose(3, 2, 1, 0)\
        .reshape(DENSE, BATCH)
    arrays["w1"] = np.asarray(inputs["W_top1"])[np.array(pair_rows())]
    arrays["b1"] = np.asarray(inputs["b_top1"]).reshape(OUT1, P).T
    arrays["w2"] = inputs["W_top2"]
    arrays["b2"] = np.asarray(inputs["b_top2"]).reshape(OUT2, P).T
    arrays["w3"] = np.asarray(inputs["W_top3"]).reshape(OUT2, P).T

    nc = bacc.Bacc("TRN2", target_bir_lowering=False, num_devices=1)
    feeds, aps = {}, {}
    for name, a in arrays.items():
        a = np.ascontiguousarray(a)
        feeds[f"in_{name}"] = a
        aps[name] = nc.dram_tensor(f"in_{name}", a.shape, mybir.dt.from_np(a.dtype), kind="ExternalInput").ap()
    out = nc.dram_tensor("out_y", (BATCH, 1), F32, kind="ExternalOutput").ap()
    build(nc, aps["ids"], aps["dense"], [aps[f"tbl_{f}"] for f in range(FEATURES)], aps["w1"], aps["b1"],
          aps["w2"], aps["b2"], aps["w3"], out)
    result = run_bass_kernel_spmd(nc, [feeds], core_ids=[0])
    return result.results[0]["out_y"]
```

```python
from contextlib import ExitStack

import concourse.bass as bass
from concourse import mybir

F32 = mybir.dt.float32
F32R = mybir.dt.float32r
F16 = mybir.dt.float16
I32 = mybir.dt.int32
I16 = mybir.dt.int16
ALU = mybir.AluOpType
ACT = mybir.ActivationFunctionType

P = 128
BATCH = 512
DIM = 128
FEATURES = 27
DENSE = 16
HIDDEN1 = 512
HIDDEN2 = 256
TILES = BATCH // P
QUAD = 4
QUADS = P // QUAD

ROWS = [1000, 12500, 1250, 1250, 12500, 125000, 1250, 1250, 1250, 1000, 1000, 1250, 1250, 1000, 1000, 12500,
        1250, 1250, 1250, 12500, 1000, 12500, 1000, 12500, 1000, 1000, 1250]
PICK_ROWS = 1000
GATHER_FEATURES = [f for f in range(FEATURES) if ROWS[f] != PICK_ROWS]
PICK_FEATURES = [f for f in range(FEATURES) if ROWS[f] == PICK_ROWS]
SLOT_FEATURE = PICK_FEATURES + GATHER_FEATURES
GATHERED = len(GATHER_FEATURES)
PICKED = len(PICK_FEATURES)

TURN = 4
TURN_SLOTS = [range(a, min(a + TURN, FEATURES)) for a in range(PICKED, FEATURES, TURN)]
TURNS = len(TURN_SLOTS)

CHUNKS = 8
PICK_PART = PICK_ROWS // CHUNKS
SPRAY = PICK_PART // 16 * 16
IDS_SLOTS = 4
SPLITS = 3
LAST = TILES - 1
HOT_SLOTS = 2 * CHUNKS

STEPS = (FEATURES - 1) // 2
WIDE = FEATURES + STEPS
GRAM_QUADS = 8
GRAMS = QUADS // GRAM_QUADS
PAIR_N = 9
PAIR_CHUNKS = FEATURES // PAIR_N
PAIR_PART = PAIR_N * STEPS
DENSE_FIRST = P - PAIR_PART
K_ROWS = [P, PAIR_PART + DENSE - DENSE_FIRST, PAIR_PART]
OUT1 = HIDDEN1 // P
OUT2 = HIDDEN2 // P


def plan():
    order = []

    def ids(*features):
        order.extend(("ids", i, 0) for i in features if i < PICKED)

    def onehot(i):
        order.append(("onehot", i, 0))

    def turn(t, *groups):
        order.extend(("turn", t, g) for g in groups)

    def gram(t):
        order.extend(("gram", t, j) for j in range(GRAMS))

    def mlp(t):
        order.extend([("layer1", t, 0), ("layer2", t, 0), ("layer3", t, 0)])

    ids(0, 1, 2)
    for i in range(PICKED):
        onehot(i)
        ids(i + 3)
        if 1 <= i <= TURNS:
            turn(0, i - 1)
        elif i > TURNS:
            turn(1, i - TURNS - 1)
    gram(0)
    turn(1, 3, 4)
    gram(1)
    turn(2, 0, 1, 2)
    mlp(0)
    turn(2, 3, 4)
    gram(2)
    turn(3, 0, 1)
    mlp(1)
    turn(3, 2, 3, 4)
    gram(3)
    order.append(("layer1", 2, 0))
    order.append(("square", LAST, 0))
    order.append(("layer2", 2, 0))
    order.append(("fold", LAST, 0))
    order.append(("layer3", 2, 0))
    mlp(3)
    return order


def build(nc, ids, dense, tables, w1, b1, w2, b2, w3, out):
    order = plan()
    turn_use = {s: n for n, s in enumerate(s for s in order if s[0] in ("ids", "turn", "fold"))}
    acc_use = {s: n for n, s in enumerate(s for s in order if s[0] in ("onehot", "layer1", "layer2", "layer3"))}
    gram_use = {s: n for n, s in enumerate(s for s in order if s[0] == "gram")}

    with ExitStack() as ctx:
        def sb(name, shape, dt=F32):
            return ctx.enter_context(nc.sbuf_tensor(name, shape, dt))

        def ps(name, shape):
            return ctx.enter_context(nc.psum_tensor(name, shape, F32))

        def sem(name):
            return ctx.enter_context(nc.semaphore(name))

        ids_sb = sb("ids_sb", [P, TILES * FEATURES], I32)
        ids_h = sb("ids_h", [P, TILES * FEATURES], F16)
        identity = sb("identity", [P, P])
        identity_h = sb("identity_h", [P, P], F16)
        row_number_i = sb("row_number_i", [P, CHUNKS], I32)
        row_number = sb("row_number", [P, CHUNKS])
        ids_rows = sb("ids_rows", [P, IDS_SLOTS, BATCH], I16)
        raw = sb("raw", [P, TILES, GATHERED, DIM])
        table = sb("table", [PICK_PART, 2, CHUNKS * DIM])
        table_hi = sb("table_hi", [PICK_PART, SPLITS, CHUNKS * DIM], F32R)
        table_lo = sb("table_lo", [PICK_PART, SPLITS, CHUNKS * DIM], F32R)
        hot = sb("hot", [PICK_PART, HOT_SLOTS, BATCH], F32R)
        vec = sb("vec", [DIM, TILES, P, 32])
        dots = sb("dots", [32, FEATURES, QUAD, QUADS])
        z = sb("z", [P, PAIR_CHUNKS * PAIR_PART])
        pairs = sb("pairs", [P, PAIR_CHUNKS, BATCH])
        w1_sb = sb("w1_sb", [P, PAIR_CHUNKS, HIDDEN1])
        w2_sb = sb("w2_sb", [P, OUT1, HIDDEN2])
        w3_sb = sb("w3_sb", [P, OUT2])
        b1_sb = sb("b1_sb", [P, OUT1])
        b2_sb = sb("b2_sb", [P, OUT2])
        h1 = sb("h1", [P, OUT1, P])
        h2 = sb("h2", [P, OUT2, P])
        y = sb("y", [1, BATCH])

        turn_ps = ps("turn_ps", [P, 2, TURN, P])
        acc_ps = ps("acc_ps", [P, 2, 512])
        gram_ps = ps("gram_ps", [P, 2, GRAM_QUADS, P])
        square_ps = gram_ps[:, :, :, :].rearrange("p b q c -> p (b q c)")[:, 0:WIDE * 32]

        scratch = nc.dram_tensor("scratch", [TILES, FEATURES, WIDE * P], F32, kind="Internal").ap()

        ids_in = sem("ids_in")
        table_in = [sem(f"table_in{r}") for r in range(2)]
        weights_in = sem("weights_in")
        dense_in = sem("dense_in")
        rows_in = [[sem(f"rows_in{t}_{g}") for g in range(TURNS)] for t in range(TILES)]
        dots_out = sem("dots_out")
        pairs_in = [sem(f"pairs_in{t}") for t in range(LAST)]
        y_out = sem("y_out")
        zeroed = sem("zeroed")
        identity_made = sem("identity_made")
        rows_numbered = sem("rows_numbered")
        ids_float = sem("ids_float")
        numbers_float = sem("numbers_float")
        padded = sem("padded")
        hi_made = sem("hi_made")
        lo_made = sem("lo_made")
        hot_made = sem("hot_made")
        hot_used = sem("hot_used")
        turned = sem("turned")
        turn_read = sem("turn_read")
        acc_done = sem("acc_done")
        acc_read = sem("acc_read")
        gram_done = sem("gram_done")
        square_done = sem("square_done")
        z_made = sem("z_made")
        gram_read_act = sem("gram_read_act")
        gram_read_dve = sem("gram_read_dve")

        block = ctx.enter_context(nc.Block())

        def gram_read(s, use):
            return gram_ps[32 * s:32 * s + 32, use % 2, :, s * FEATURES:(s + 1) * FEATURES].rearrange("n q m -> n m q")

        def dots_at(s, j):
            return dots[:, :, s, j * GRAM_QUADS:(j + 1) * GRAM_QUADS]

        @block.sync
        def _(sp):
            def load_table(i):
                if i >= 2:
                    sp.wait_ge(lo_made, i - 1)
                src = tables[PICK_FEATURES[i]].rearrange("(p c) d -> p (c d)", c=CHUNKS)
                for a, b in ((0, SPRAY), (SPRAY, PICK_PART)):
                    sp.dma_start(table[a:b, i % 2, :], src[a:b, :]).then_inc(table_in[i % 2], 16)

            sp.dma_start(ids_sb[:, :], ids.rearrange("(p t) f -> p (t f)", t=TILES)).then_inc(ids_in, 16)
            for i in range(4):
                load_table(i)
            row = 0
            for c, k in enumerate(K_ROWS):
                sp.dma_start(w1_sb[0:k, c, :], w1[row:row + k, :]).then_inc(weights_in, 16)
                row += k
            sp.dma_start(w2_sb[:, :, :], w2.rearrange("(c p) n -> p c n", p=P)).then_inc(weights_in, 16)
            sp.dma_start(w3_sb[:, :], w3).then_inc(weights_in, 16)
            sp.dma_start(b1_sb[:, :], b1).then_inc(weights_in, 16)
            sp.dma_start(b2_sb[:, :], b2).then_inc(weights_in, 16)
            sp.dma_start(pairs[PAIR_PART:P, 0, :], dense[0:DENSE_FIRST, :]).then_inc(dense_in, 16)
            sp.dma_start(pairs[PAIR_PART:K_ROWS[1], 1, :], dense[DENSE_FIRST:DENSE, :]).then_inc(dense_in, 16)
            for i in range(4, PICKED):
                load_table(i)

            for t in range(LAST):
                sp.wait_ge(gram_read_act, GRAMS * (t + 1))
                sp.wait_ge(gram_read_dve, GRAMS * (t + 1))
                here = dots[0:FEATURES, :, :, :].rearrange("n m s q -> n (m s q)")
                sp.dma_start(scratch[t, :, 0:FEATURES * P], here).then_inc(dots_out, 16)
                sp.dma_start(scratch[t, :, FEATURES * P:], here[:, 0:STEPS * P]).then_inc(dots_out, 16)
                sp.wait_ge(dots_out, 32 * (t + 1))
                row_len = WIDE * P
                for c in range(PAIR_CHUNKS):
                    first = scratch[t, :, :]
                    n0 = c * PAIR_N
                    src = bass.AP(first.tensor, first.offset + n0 * row_len + (n0 + 1) * P,
                                  [[row_len + P, PAIR_N], [P, STEPS], [1, P]])
                    sp.dma_start(pairs[0:PAIR_PART, c, t * P:(t + 1) * P], src).then_inc(pairs_in[t], 16)

            sp.wait_ge(acc_read, acc_use["layer3", LAST, 0] + 1)
            sp.dma_start(out.rearrange("b o -> o b"), y[:, :]).then_inc(y_out, 16)
            sp.wait_ge(y_out, 16)

        @block.gpsimd
        def _(pool):
            pool.memset(identity[:, :], 0.0).then_inc(zeroed, 1)
            pool.iota(row_number_i[:, :], pattern=[[1, CHUNKS]], base=0, channel_multiplier=CHUNKS)\
                .then_inc(rows_numbered, 1)
            pool.wait_ge(zeroed, 1)
            pool.affine_select(out=identity[:, :], in_=identity[:, :], compare_op=ALU.not_equal, fill=1.0,
                               base=0, pattern=[[-1, P]], channel_multiplier=1).then_inc(identity_made, 1)
            pool.wait_ge(ids_in, 16)
            for t in range(TILES):
                for g, slots in enumerate(TURN_SLOTS):
                    for n in slots:
                        f = SLOT_FEATURE[n]
                        at = t * FEATURES + f
                        pool.indirect_dma_start(raw[:, t, n - PICKED, :], None, tables[f],
                                                bass.IndirectOffsetOnAxis(ap=ids_sb[:, at:at + 1], axis=0))\
                            .then_inc(rows_in[t][g], 16)

        @block.tensor
        def _(pe):
            for step in order:
                kind, t, g = step
                if kind in ("ids", "turn", "fold"):
                    use = turn_use[step]
                    bank = turn_ps[:, use % 2, :, :]
                    if use >= 2:
                        pe.wait_ge(turn_read, use - 1)
                    if kind == "ids":
                        if use == 0:
                            pe.wait_ge(ids_float, 2)
                        for tile in range(TILES):
                            at = tile * FEATURES + PICK_FEATURES[t]
                            last = pe.matmul(bank[:, tile, :], ids_h[:, at:at + 1].broadcast_to([P, P]),
                                             identity_h[:, :], start=True, stop=True)
                    elif kind == "fold":
                        pe.wait_ge(z_made, 1)
                        for c in range(PAIR_CHUNKS):
                            last = pe.transpose(bank[0:PAIR_PART, c, :], z[:, c * PAIR_PART:(c + 1) * PAIR_PART],
                                                identity[:, :])
                    else:
                        slots = TURN_SLOTS[g]
                        pe.wait_ge(rows_in[t][g], 16 * len(slots))
                        pe.wait_ge(identity_made, 1)
                        for x, n in enumerate(slots):
                            last = pe.transpose(bank[:, x, :], raw[:, t, n - PICKED, :], identity[:, :])
                    last.then_inc(turned, 1)
                    continue
                if kind == "gram":
                    use = gram_use[step]
                    if g == 0:
                        pe.wait_ge(turn_read, turn_use["turn", t, TURNS - 1] + 1)
                        pe.wait_ge(acc_read, acc_use["onehot", PICKED - 1, 0] + 1)
                        if t == 0:
                            pe.wait_ge(padded, 1)
                    if use >= 2:
                        pe.wait_ge(gram_read_act, use - 1)
                        pe.wait_ge(gram_read_dve, use - 1)
                    for x in range(GRAM_QUADS):
                        q = g * GRAM_QUADS + x
                        quad = vec[:, t, q * QUAD:(q + 1) * QUAD, :]
                        last = pe.matmul(gram_ps[:, use % 2, x, 0:QUAD * FEATURES],
                                         quad.rearrange("d s f -> d (s f)"), quad[:, :, 0:FEATURES],
                                         start=True, stop=True)
                    last.then_inc(gram_done, 1)
                    continue
                if kind == "square":
                    pe.wait_ge(gram_read_act, GRAMS * TILES)
                    pe.wait_ge(gram_read_dve, GRAMS * TILES)
                    for m in range(1, WIDE):
                        rows = dots[0:FEATURES, m % FEATURES, :, :].rearrange("n s q -> n (s q)")
                        last = pe.transpose(square_ps[:, m * 32:m * 32 + FEATURES], rows,
                                            identity[0:FEATURES, 0:FEATURES])
                    last.then_inc(square_done, 1)
                    continue
                use = acc_use[step]
                bank = acc_ps[:, use % 2, :]
                if use >= 2:
                    pe.wait_ge(acc_read, use - 1)
                if kind == "onehot":
                    i = t
                    pe.wait_ge(hi_made, i + 1)
                    pe.wait_ge(lo_made, i + 1)
                    for c in range(CHUNKS):
                        n = i * CHUNKS + c
                        pe.wait_ge(hot_made, n + 1)
                        rows = hot[:, n % HOT_SLOTS, :]
                        pe.matmul(bank, table_hi[:, i % SPLITS, c * DIM:(c + 1) * DIM], rows,
                                  start=(c == 0), stop=False)
                        last = pe.matmul(bank, table_lo[:, i % SPLITS, c * DIM:(c + 1) * DIM], rows,
                                         start=False, stop=(c == CHUNKS - 1))
                        if c < CHUNKS - 1:
                            last.then_inc(hot_used, 1)
                        else:
                            last.then_inc(acc_done, 1)
                elif kind == "layer1":
                    if t == 0:
                        pe.wait_ge(weights_in, 7 * 16)
                        pe.wait_ge(dense_in, 2 * 16)
                    if t < LAST:
                        pe.wait_ge(pairs_in[t], PAIR_CHUNKS * 16)
                    else:
                        pe.wait_ge(turn_read, turn_use["fold", LAST, 0] + 1)
                    for o in range(OUT1):
                        for c, k in enumerate(K_ROWS):
                            last = pe.matmul(bank[:, o * P:(o + 1) * P], w1_sb[0:k, c, o * P:(o + 1) * P],
                                             pairs[0:k, c, t * P:(t + 1) * P],
                                             start=(c == 0), stop=(c == PAIR_CHUNKS - 1))
                    last.then_inc(acc_done, 1)
                elif kind == "layer2":
                    pe.wait_ge(acc_read, acc_use["layer1", t, 0] + 1)
                    for o in range(OUT2):
                        for c in range(OUT1):
                            last = pe.matmul(bank[:, o * P:(o + 1) * P], w2_sb[:, c, o * P:(o + 1) * P],
                                             h1[:, c, :], start=(c == 0), stop=(c == OUT1 - 1))
                    last.then_inc(acc_done, 1)
                else:
                    pe.wait_ge(acc_read, acc_use["layer2", t, 0] + 1)
                    for c in range(OUT2):
                        last = pe.matmul(bank[0:1, 0:P], w3_sb[:, c:c + 1], h2[:, c, :],
                                         start=(c == 0), stop=(c == OUT2 - 1))
                    last.then_inc(acc_done, 1)

        @block.scalar
        def _(act):
            def split_hi(i):
                act.wait_ge(table_in[i % 2], 32 * (i // 2 + 1))
                if i >= SPLITS:
                    act.wait_ge(acc_done, acc_use["onehot", i - SPLITS, 0] + 1)
                act.copy(table_hi[:, i % SPLITS, :], table[:, i % 2, :]).then_inc(hi_made, 1)

            split_hi(0)
            split_hi(1)
            for step in order:
                kind, t, g = step
                if kind == "ids":
                    use = turn_use[step]
                    act.wait_ge(turned, use + 1)
                    if t >= IDS_SLOTS:
                        act.wait_ge(hot_made, CHUNKS * (t - IDS_SLOTS + 1))
                    act.copy(ids_rows[:, t % IDS_SLOTS, :], turn_ps[:, use % 2, :, :].rearrange("p t b -> p (t b)"))\
                       .then_inc(turn_read, 1)
                elif kind == "turn":
                    use = turn_use[step]
                    slots = TURN_SLOTS[g]
                    act.wait_ge(turned, use + 1)
                    act.copy(vec[:, t, :, slots.start:slots.stop], turn_ps[:, use % 2, 0:len(slots), :].rearrange("d f p -> d p f"))\
                       .then_inc(turn_read, 1)
                elif kind == "fold":
                    use = turn_use[step]
                    act.wait_ge(turned, use + 1)
                    act.copy(pairs[0:PAIR_PART, :, LAST * P:], turn_ps[0:PAIR_PART, use % 2, 0:PAIR_CHUNKS, :])\
                       .then_inc(turn_read, 1)
                elif kind == "onehot":
                    i = t
                    if i + 2 < PICKED:
                        split_hi(i + 2)
                    use = acc_use[step]
                    act.wait_ge(acc_done, use + 1)
                    act.copy(vec[:, :, :, i], acc_ps[:, use % 2, :].rearrange("d (t p) -> d t p", t=TILES))\
                       .then_inc(acc_read, 1)
                elif kind == "gram":
                    use = gram_use[step]
                    if g == 0 and t >= 1:
                        act.wait_ge(dots_out, 32 * t)
                    act.wait_ge(gram_done, use + 1)
                    for s in (0, 1):
                        last = act.copy(dots_at(s, g), gram_read(s, use))
                    last.then_inc(gram_read_act, 1)
                elif kind == "square":
                    continue
                elif kind == "layer1":
                    use = acc_use[step]
                    if t == 0:
                        act.wait_ge(weights_in, 7 * 16)
                    act.wait_ge(acc_done, use + 1)
                    for o in range(OUT1):
                        last = act.activation(h1[:, o, :], acc_ps[:, use % 2, o * P:(o + 1) * P], ACT.Relu,
                                              bias=b1_sb[:, o:o + 1])
                    last.then_inc(acc_read, 1)
                elif kind == "layer2":
                    use = acc_use[step]
                    act.wait_ge(acc_done, use + 1)
                    for o in range(OUT2):
                        last = act.activation(h2[:, o, :], acc_ps[:, use % 2, o * P:(o + 1) * P], ACT.Relu,
                                              bias=b2_sb[:, o:o + 1])
                    last.then_inc(acc_read, 1)
                else:
                    use = acc_use[step]
                    act.wait_ge(acc_done, use + 1)
                    dst = y[:, :].rearrange("o (q s t) -> o s q t", s=QUAD, t=TILES)[:, :, :, t]
                    act.copy(dst, acc_ps[0:1, use % 2, 0:P].rearrange("o (s q) -> o s q", s=QUAD))\
                       .then_inc(acc_read, 1)

        @block.vector
        def _(dve):
            def make_hot(i):
                dve.wait_ge(turn_read, turn_use["ids", i, 0] + 1)
                for c in range(CHUNKS):
                    if i >= 2:
                        if c < CHUNKS - 1:
                            dve.wait_ge(hot_used, (i - 2) * (CHUNKS - 1) + c + 1)
                        else:
                            dve.wait_ge(acc_done, acc_use["onehot", i - 2, 0] + 1)
                    dve.tensor_scalar(hot[:, (i * CHUNKS + c) % HOT_SLOTS, :], ids_rows[0:PICK_PART, i % IDS_SLOTS, :],
                                      row_number[0:PICK_PART, c:c + 1], None, ALU.is_equal).then_inc(hot_made, 1)

            def split_lo(i):
                dve.wait_ge(table_in[i % 2], 32 * (i // 2 + 1))
                dve.wait_ge(hi_made, i + 1)
                if i >= SPLITS:
                    dve.wait_ge(acc_done, acc_use["onehot", i - SPLITS, 0] + 1)
                dve.tensor_tensor(table_lo[:, i % SPLITS, :], table[:, i % 2, :],
                                  table_hi[:, i % SPLITS, :].bitcast(F32), ALU.subtract).then_inc(lo_made, 1)

            dve.memset(vec[:, :, :, FEATURES:], 0.0).then_inc(padded, 1)
            dve.wait_ge(rows_numbered, 1)
            dve.tensor_copy(row_number[:, :], row_number_i[:, :]).then_inc(numbers_float, 1)
            dve.wait_ge(ids_in, 16)
            dve.tensor_copy(ids_h[:, :], ids_sb[:, :]).then_inc(ids_float, 1)
            dve.wait_ge(identity_made, 1)
            dve.tensor_copy(identity_h[:, :], identity[:, :]).then_inc(ids_float, 1)
            dve.wait_ge(numbers_float, 1)
            split_lo(0)
            make_hot(0)
            for step in order:
                kind, t, g = step
                if kind == "onehot":
                    if t + 1 < PICKED:
                        split_lo(t + 1)
                        make_hot(t + 1)
                elif kind == "gram":
                    use = gram_use[step]
                    if g == 0 and t >= 1:
                        dve.wait_ge(dots_out, 32 * t)
                    dve.wait_ge(gram_done, use + 1)
                    for s in (2, 3):
                        last = dve.tensor_copy(dots_at(s, g), gram_read(s, use))
                    last.then_inc(gram_read_dve, 1)
                elif kind == "square":
                    dve.wait_ge(square_done, 1)
                    first = square_ps[:, 32:]
                    src = bass.AP(first.tensor, first.offset, [first.ap[0], [33, FEATURES], [32, STEPS]])
                    dve.tensor_copy(z[:, :].rearrange("p (n k) -> p n k", k=STEPS), src).then_inc(z_made, 1)


def pair_rows():
    dense_row = FEATURES * (FEATURES - 1) // 2
    rows = []
    for c in range(PAIR_CHUNKS):
        for n in range(c * PAIR_N, (c + 1) * PAIR_N):
            for k in range(1, STEPS + 1):
                i, j = sorted((SLOT_FEATURE[n], SLOT_FEATURE[(n + k) % FEATURES]))
                rows.append(j * (j - 1) // 2 + i)
        extra = K_ROWS[c] - PAIR_PART
        rows += range(dense_row, dense_row + extra)
        dense_row += extra
    return rows


def kernel(**inputs):
    import numpy as np
    import concourse.bacc as bacc
    from concourse.bass_utils import run_bass_kernel_spmd

    arrays = {"ids": inputs["ids"]}
    for f in range(FEATURES):
        arrays[f"tbl_{f}"] = inputs[f"tbl_{f}"]
    arrays["dense"] = np.asarray(inputs["dense_ctx"]).reshape(QUADS, QUAD, TILES, DENSE).transpose(3, 2, 1, 0)\
        .reshape(DENSE, BATCH)
    arrays["w1"] = np.asarray(inputs["W_top1"])[np.array(pair_rows())]
    arrays["b1"] = np.asarray(inputs["b_top1"]).reshape(OUT1, P).T
    arrays["w2"] = inputs["W_top2"]
    arrays["b2"] = np.asarray(inputs["b_top2"]).reshape(OUT2, P).T
    arrays["w3"] = np.asarray(inputs["W_top3"]).reshape(OUT2, P).T

    nc = bacc.Bacc("TRN2", target_bir_lowering=False, num_devices=1)
    feeds, aps = {}, {}
    for name, a in arrays.items():
        a = np.ascontiguousarray(a)
        feeds[f"in_{name}"] = a
        aps[name] = nc.dram_tensor(f"in_{name}", a.shape, mybir.dt.from_np(a.dtype), kind="ExternalInput").ap()
    out = nc.dram_tensor("out_y", (BATCH, 1), F32, kind="ExternalOutput").ap()
    build(nc, aps["ids"], aps["dense"], [aps[f"tbl_{f}"] for f in range(FEATURES)], aps["w1"], aps["b1"],
          aps["w2"], aps["b2"], aps["w3"], out)
    result = run_bass_kernel_spmd(nc, [feeds], core_ids=[0])
    return result.results[0]["out_y"]
```

```python
from contextlib import ExitStack

import concourse.bass as bass
from concourse import mybir

F32 = mybir.dt.float32
F32R = mybir.dt.float32r
F16 = mybir.dt.float16
I32 = mybir.dt.int32
ALU = mybir.AluOpType
ACT = mybir.ActivationFunctionType

P = 128
BATCH = 512
DIM = 128
FEATURES = 27
DENSE = 16
HIDDEN1 = 512
HIDDEN2 = 256
TILES = BATCH // P
QUAD = 4
QUADS = P // QUAD

ROWS = [1000, 12500, 1250, 1250, 12500, 125000, 1250, 1250, 1250, 1000, 1000, 1250, 1250, 1000, 1000, 12500,
        1250, 1250, 1250, 12500, 1000, 12500, 1000, 12500, 1000, 1000, 1250]
PICK_ROWS = 1000
GATHER_FEATURES = [f for f in range(FEATURES) if ROWS[f] != PICK_ROWS]
PICK_FEATURES = [f for f in range(FEATURES) if ROWS[f] == PICK_ROWS]
SLOT_FEATURE = PICK_FEATURES + GATHER_FEATURES
GATHERED = len(GATHER_FEATURES)
PICKED = len(PICK_FEATURES)

TURN = 4
TURN_SLOTS = [range(a, min(a + TURN, FEATURES)) for a in range(PICKED, FEATURES, TURN)]
TURNS = len(TURN_SLOTS)

CHUNKS = 8
PICK_PART = PICK_ROWS // CHUNKS
SPRAY = PICK_PART // 16 * 16
RAWS = 3
IDS_SLOTS = 3
SPLITS = 3
LAST = TILES - 1
WARM_UP = 14
DVE_BLOCKS = CHUNKS - 1
FIRST_HOT = 5
HOT_SLOTS = 2 * CHUNKS

STEPS = (FEATURES - 1) // 2
WIDE = FEATURES + STEPS
GRAM_QUADS = 8
GRAMS = QUADS // GRAM_QUADS
QUAD_COLUMNS = (QUAD - 1) * 32 + FEATURES
SQUARE_M = 2 * 512 // 32
PAIR_N = 9
PAIR_CHUNKS = FEATURES // PAIR_N
PAIR_PART = PAIR_N * STEPS
DENSE_FIRST = P - PAIR_PART
K_ROWS = [P, PAIR_PART + DENSE - DENSE_FIRST, PAIR_PART]
OUT1 = HIDDEN1 // P
OUT2 = HIDDEN2 // P
WEIGHT_LOADS = PAIR_CHUNKS + 4


def plan():
    order = []

    def onehot(i):
        order.append(("onehot", i, 0))

    def turn(t, *groups):
        order.extend(("turn", t, g) for g in groups)

    def gram(t, *groups):
        order.extend(("gram", t, j) for j in groups)

    def square(part):
        order.append(("square", LAST, part))

    def layer1(t, *outputs):
        order.extend(("layer1", t, o) for o in outputs or range(OUT1))

    def layer2(t, *outputs):
        order.extend(("layer2", t, o) for o in outputs or range(OUT2))

    def layer3(t):
        order.append(("layer3", t, 0))

    early = [(t, g) for t in (0, 1) for g in range(TURNS)][:PICKED - 1]
    for i in range(PICKED):
        onehot(i)
        if i >= 1:
            turn(early[i - 1][0], early[i - 1][1])
    turn(1, *range(PICKED - 1 - TURNS, TURNS))
    gram(0, 0, 1, 2, 3)
    turn(2, 0, 1)
    gram(1, 0, 1, 2)
    turn(2, 2)
    gram(1, 3)
    layer1(0)
    turn(2, 3, 4)
    layer2(0, 0)
    gram(2, 0, 1, 2, 3)
    layer2(0, 1)
    layer1(1)
    layer3(0)
    turn(3, 0)
    layer2(1)
    turn(3, 1, 2)
    layer3(1)
    turn(3, 3)
    layer1(2, 0, 1)
    turn(3, 4)
    layer1(2, 2)
    gram(3, 0, 1, 2, 3)
    layer1(2, 3)
    square(0)
    square(1)
    layer2(2, 0)
    order.append(("fold", LAST, 0))
    layer2(2, 1)
    layer1(3)
    layer2(3)
    layer3(2)
    layer3(3)
    return order


def build(nc, ids, pick_ids, dense, tables, w1, b1, w2, b2, w3, out):
    order = plan()
    turn_use = {s: n for n, s in enumerate(s for s in order if s[0] in ("turn", "fold"))}
    acc_use = {s: n for n, s in enumerate(s for s in order if s[0] in ("onehot", "layer1", "layer2", "layer3"))}
    gram_use = {s: n for n, s in enumerate(s for s in order if s[0] == "gram")}

    with ExitStack() as ctx:
        def sb(name, shape, dt=F32):
            return ctx.enter_context(nc.sbuf_tensor(name, shape, dt))

        def ps(name, shape):
            return ctx.enter_context(nc.psum_tensor(name, shape, F32))

        def sem(name):
            return ctx.enter_context(nc.semaphore(name))

        ids_sb = sb("ids_sb", [P, TILES * FEATURES], I32)
        identity = sb("identity", [P, P])
        row_number_i = sb("row_number_i", [P, CHUNKS], I32)
        row_number = sb("row_number", [P, CHUNKS])
        minus_row = sb("minus_row", [P, 1])
        away = sb("away", [PICK_PART, BATCH], F16)
        ids_rows = sb("ids_rows", [PICK_PART, IDS_SLOTS, BATCH], I32)
        raw = sb("raw", [P, RAWS, GATHERED, DIM])
        table = sb("table", [P, 2, CHUNKS * DIM])
        table_hi = sb("table_hi", [PICK_PART, SPLITS, CHUNKS * DIM], F32R)
        table_lo = sb("table_lo", [PICK_PART, SPLITS, CHUNKS * DIM], F32R)
        hot = sb("hot", [PICK_PART, HOT_SLOTS, BATCH], F32R)
        vec = sb("vec", [DIM, TILES, P, 32])
        dots = sb("dots", [32, 2, FEATURES, QUAD, QUADS])
        z = sb("z", [P, PAIR_CHUNKS * PAIR_PART])
        pairs = sb("pairs", [P, PAIR_CHUNKS, BATCH])
        w1_sb = sb("w1_sb", [P, PAIR_CHUNKS, HIDDEN1])
        w2_sb = sb("w2_sb", [P, OUT1, HIDDEN2])
        w3_sb = sb("w3_sb", [P, OUT2])
        b1_sb = sb("b1_sb", [P, OUT1])
        b2_sb = sb("b2_sb", [P, OUT2])
        h1 = table[:, 0, 0:HIDDEN1].rearrange("p (o b) -> p o b", o=OUT1)
        h2 = table[:, 0, HIDDEN1:HIDDEN1 + 2 * HIDDEN2].rearrange("p (r o b) -> p r o b", r=2, o=OUT2)
        y = table[0:1, 1, 0:BATCH]

        turn_ps = ps("turn_ps", [P, 2, TURN, P])
        acc_ps = ps("acc_ps", [P, 2, 512])
        gram_ps = ps("gram_ps", [P, 2, GRAM_QUADS, P])
        square_ps = gram_ps[:, :, :, :].rearrange("p b q c -> p (b q c)")[:, 0:WIDE * 32]

        scratch = nc.dram_tensor("scratch", [TILES, FEATURES, WIDE * P], F32, kind="Internal").ap()

        ids_in = sem("ids_in")
        pick_ids_in = [sem(f"pick_ids_in{r}") for r in range(IDS_SLOTS)]
        table_in = [sem(f"table_in{r}") for r in range(2)]
        weights_in = sem("weights_in")
        dense_in = sem("dense_in")
        rows_in = [[sem(f"rows_in{t}_{g}") for g in range(TURNS)] for t in range(TILES)]
        dots_out = sem("dots_out")
        pairs_in = [sem(f"pairs_in{t}") for t in range(LAST)]
        y_out = sem("y_out")
        zeroed = sem("zeroed")
        identity_made = sem("identity_made")
        rows_numbered = sem("rows_numbered")
        numbers_float = sem("numbers_float")
        padded = sem("padded")
        hi_made = sem("hi_made")
        lo_made = sem("lo_made")
        away_made = sem("away_made")
        hot_made = sem("hot_made")
        last_hot_made = sem("last_hot_made")
        hot_used = sem("hot_used")
        turned = sem("turned")
        turn_read = sem("turn_read")
        acc_done = sem("acc_done")
        acc_read = sem("acc_read")
        gram_done = sem("gram_done")
        square_done = sem("square_done")
        z_made = sem("z_made")
        gram_read_act = sem("gram_read_act")
        gram_read_dve = sem("gram_read_dve")

        block = ctx.enter_context(nc.Block())

        def gram_read(s, use):
            return gram_ps[32 * s:32 * s + FEATURES, use % 2, :, s * FEATURES:(s + 1) * FEATURES]\
                .rearrange("n q m -> n m q")

        def dots_at(t, s, j):
            return dots[0:FEATURES, t % 2, :, s, j * GRAM_QUADS:(j + 1) * GRAM_QUADS]

        @block.sync
        def _(sp):
            def load_table(i):
                if i >= 2:
                    sp.wait_ge(lo_made, i - 1)
                src = tables[PICK_FEATURES[i]].rearrange("(p c) d -> p (c d)", c=CHUNKS)
                for a, b in ((0, SPRAY), (SPRAY, PICK_PART)):
                    sp.dma_start(table[a:b, i % 2, :], src[a:b, :]).then_inc(table_in[i % 2], 16)

            def load_ids(i):
                if i >= IDS_SLOTS:
                    sp.wait_ge(hot_made, DVE_BLOCKS * (i - IDS_SLOTS + 1))
                    sp.wait_ge(last_hot_made, i - IDS_SLOTS + 1)
                sp.dma_start(ids_rows[:, i % IDS_SLOTS, :], pick_ids[i:i + 1, :].partition_broadcast(PICK_PART))\
                    .then_inc(pick_ids_in[i % IDS_SLOTS], 16)

            sp.dma_start(ids_sb[:, :], ids.rearrange("(p t) f -> p (t f)", t=TILES)).then_inc(ids_in, 16)
            for i in range(PICKED):
                load_ids(i)
                load_table(i)
            row = 0
            for c, k in enumerate(K_ROWS):
                sp.dma_start(w1_sb[0:k, c, :], w1[row:row + k, :]).then_inc(weights_in, 16)
                row += k
            sp.dma_start(w2_sb[:, :, :], w2.rearrange("(c p) n -> p c n", p=P)).then_inc(weights_in, 16)
            sp.dma_start(w3_sb[:, :], w3).then_inc(weights_in, 16)
            sp.dma_start(b1_sb[:, :], b1).then_inc(weights_in, 16)
            sp.dma_start(b2_sb[:, :], b2).then_inc(weights_in, 16)
            sp.dma_start(pairs[PAIR_PART:P, 0, :], dense[0:DENSE_FIRST, :]).then_inc(dense_in, 16)
            sp.dma_start(pairs[PAIR_PART:K_ROWS[1], 1, :], dense[DENSE_FIRST:DENSE, :]).then_inc(dense_in, 16)

            for t in range(LAST):
                sp.wait_ge(gram_read_act, GRAMS * (t + 1))
                sp.wait_ge(gram_read_dve, GRAMS * (t + 1))
                here = dots[0:FEATURES, t % 2, :, :, :].rearrange("n m s q -> n (m s q)")
                sp.dma_start(scratch[t, :, 0:FEATURES * P], here).then_inc(dots_out, 16)
                sp.dma_start(scratch[t, :, FEATURES * P:], here[:, 0:STEPS * P]).then_inc(dots_out, 16)
                sp.wait_ge(dots_out, 32 * (t + 1))
                row_len = WIDE * P
                for c in range(PAIR_CHUNKS):
                    first = scratch[t, :, :]
                    n0 = c * PAIR_N
                    src = bass.AP(first.tensor, first.offset + n0 * row_len + (n0 + 1) * P,
                                  [[row_len + P, PAIR_N], [P, STEPS], [1, P]])
                    sp.dma_start(pairs[0:PAIR_PART, c, t * P:(t + 1) * P], src).then_inc(pairs_in[t], 16)

            sp.wait_ge(acc_read, acc_use["layer3", LAST, 0] + 1)
            sp.dma_start(out.rearrange("b o -> o b"), y[:, :]).then_inc(y_out, 16)
            sp.wait_ge(y_out, 16)

        @block.gpsimd
        def _(pool):
            pool.memset(identity[:, :], 0.0).then_inc(zeroed, 1)
            pool.iota(row_number_i[:, :], pattern=[[1, CHUNKS]], base=0, channel_multiplier=CHUNKS)\
                .then_inc(rows_numbered, 1)
            pool.wait_ge(zeroed, 1)
            pool.affine_select(out=identity[:, :], in_=identity[:, :], compare_op=ALU.not_equal, fill=1.0,
                               base=0, pattern=[[-1, P]], channel_multiplier=1).then_inc(identity_made, 1)
            pool.wait_ge(ids_in, 16)
            for t in range(TILES):
                for g, slots in enumerate(TURN_SLOTS):
                    if t >= RAWS:
                        pool.wait_ge(turned, turn_use["turn", t - RAWS, g] + 1)
                    for n in slots:
                        f = SLOT_FEATURE[n]
                        at = t * FEATURES + f
                        pool.indirect_dma_start(raw[:, t % RAWS, n - PICKED, :], None, tables[f],
                                                bass.IndirectOffsetOnAxis(ap=ids_sb[:, at:at + 1], axis=0))\
                            .then_inc(rows_in[t][g], 16)

        @block.tensor
        def _(pe):
            def warm_up(times):
                for _ in range(times):
                    pe.matmul(acc_ps[:, 1, 0:P], identity[:, :], identity[:, :], start=True, stop=True)

            pe.wait_ge(identity_made, 1)
            warm_up(WARM_UP)
            for step in order:
                kind, t, g = step
                if kind in ("turn", "fold"):
                    use = turn_use[step]
                    bank = turn_ps[:, use % 2, :, :]
                    if use >= 2:
                        pe.wait_ge(turn_read, use - 1)
                    if kind == "fold":
                        pe.wait_ge(z_made, 2)
                        for c in range(PAIR_CHUNKS):
                            last = pe.transpose(bank[0:PAIR_PART, c, :], z[:, c * PAIR_PART:(c + 1) * PAIR_PART],
                                                identity[:, :])
                    else:
                        slots = TURN_SLOTS[g]
                        pe.wait_ge(rows_in[t][g], 16 * len(slots))
                        for x, n in enumerate(slots):
                            last = pe.transpose(bank[:, x, :], raw[:, t % RAWS, n - PICKED, :], identity[:, :])
                    last.then_inc(turned, 1)
                    continue
                if kind == "gram":
                    use = gram_use[step]
                    if g == 0:
                        pe.wait_ge(turn_read, turn_use["turn", t, TURNS - 1] + 1)
                        pe.wait_ge(acc_read, acc_use["onehot", PICKED - 1, 0] + 1)
                        if t == 0:
                            pe.wait_ge(padded, 1)
                    if use >= 2:
                        pe.wait_ge(gram_read_act, use - 1)
                        pe.wait_ge(gram_read_dve, use - 1)
                    for x in range(GRAM_QUADS):
                        q = g * GRAM_QUADS + x
                        quad = vec[:, t, q * QUAD:(q + 1) * QUAD, :]
                        last = pe.matmul(gram_ps[0:QUAD_COLUMNS, use % 2, x, 0:QUAD * FEATURES],
                                         quad.rearrange("d s f -> d (s f)")[:, 0:QUAD_COLUMNS], quad[:, :, 0:FEATURES],
                                         start=True, stop=True)
                    last.then_inc(gram_done, 1)
                    continue
                if kind == "square":
                    pe.wait_ge(gram_read_act, GRAMS * TILES)
                    pe.wait_ge(gram_read_dve, GRAMS * TILES)
                    for m in range(1, SQUARE_M) if g == 0 else range(SQUARE_M, WIDE):
                        rows = dots[0:FEATURES, t % 2, m % FEATURES, :, :].rearrange("n s q -> n (s q)")
                        last = pe.transpose(square_ps[:, m * 32:m * 32 + FEATURES], rows,
                                            identity[0:FEATURES, 0:FEATURES])
                    last.then_inc(square_done, 1)
                    continue
                use = acc_use[step]
                bank = acc_ps[:, use % 2, :]
                if use >= 2:
                    pe.wait_ge(acc_read, use - 1)
                if kind == "onehot":
                    i = t
                    pe.wait_ge(hi_made, i + 1)
                    pe.wait_ge(lo_made, i + 1)
                    for c in range(CHUNKS):
                        n = i * CHUNKS + c
                        if c < DVE_BLOCKS:
                            pe.wait_ge(hot_made, i * DVE_BLOCKS + c + 1)
                        else:
                            pe.wait_ge(last_hot_made, i + 1)
                        rows = hot[:, n % HOT_SLOTS, :]
                        pe.matmul(bank, table_hi[:, i % SPLITS, c * DIM:(c + 1) * DIM], rows,
                                  start=(c == 0), stop=False)
                        last = pe.matmul(bank, table_lo[:, i % SPLITS, c * DIM:(c + 1) * DIM], rows,
                                         start=False, stop=(c == CHUNKS - 1))
                        if c < DVE_BLOCKS:
                            last.then_inc(hot_used, 1)
                        else:
                            last.then_inc(acc_done, 1)
                elif kind == "layer1":
                    if t == 0 and g == 0:
                        pe.wait_ge(weights_in, 16 * WEIGHT_LOADS)
                        pe.wait_ge(dense_in, 2 * 16)
                    if t < LAST:
                        pe.wait_ge(pairs_in[t], PAIR_CHUNKS * 16)
                    else:
                        pe.wait_ge(turn_read, turn_use["fold", LAST, 0] + 1)
                    for c, k in enumerate(K_ROWS):
                        last = pe.matmul(bank[:, 0:P], w1_sb[0:k, c, g * P:(g + 1) * P],
                                         pairs[0:k, c, t * P:(t + 1) * P],
                                         start=(c == 0), stop=(c == PAIR_CHUNKS - 1))
                    last.then_inc(acc_done, 1)
                elif kind == "layer2":
                    for c in range(OUT1):
                        if g == 0:
                            pe.wait_ge(acc_read, acc_use["layer1", t, c] + 1)
                        last = pe.matmul(bank[:, 0:P], w2_sb[:, c, g * P:(g + 1) * P], h1[:, c, :],
                                         start=(c == 0), stop=(c == OUT1 - 1))
                    last.then_inc(acc_done, 1)
                else:
                    for c in range(OUT2):
                        pe.wait_ge(acc_read, acc_use["layer2", t, c] + 1)
                        last = pe.matmul(bank[0:1, 0:P], w3_sb[:, c:c + 1], h2[:, t % 2, c, :],
                                         start=(c == 0), stop=(c == OUT2 - 1))
                    last.then_inc(acc_done, 1)

        @block.scalar
        def _(act):
            def split_hi(i):
                act.wait_ge(table_in[i % 2], 32 * (i // 2 + 1))
                if i >= SPLITS:
                    act.wait_ge(acc_done, acc_use["onehot", i - SPLITS, 0] + 1)
                act.copy(table_hi[:, i % SPLITS, :], table[0:PICK_PART, i % 2, :]).then_inc(hi_made, 1)

            def last_block(i):
                act.wait_ge(pick_ids_in[i % IDS_SLOTS], 16 * (i // IDS_SLOTS + 1))
                if i == 0:
                    act.wait_ge(numbers_float, 2)
                else:
                    act.wait_ge(last_hot_made, i)
                act.activation(away[:, :], ids_rows[:, i % IDS_SLOTS, :], ACT.Abs,
                               bias=minus_row[0:PICK_PART, :]).then_inc(away_made, 1)
                act.wait_ge(away_made, i + 1)
                if i >= 2:
                    act.wait_ge(acc_done, acc_use["onehot", i - 2, 0] + 1)
                act.activation(hot[:, (i * CHUNKS + CHUNKS - 1) % HOT_SLOTS, :], away[:, :], ACT.Relu,
                               bias=1.0, scale=-1.0).then_inc(last_hot_made, 1)

            split_hi(0)
            last_block(0)
            split_hi(1)
            for step in order:
                kind, t, g = step
                if kind == "turn":
                    use = turn_use[step]
                    slots = TURN_SLOTS[g]
                    act.wait_ge(turned, use + 1)
                    act.copy(vec[:, t, :, slots.start:slots.stop],
                             turn_ps[:, use % 2, 0:len(slots), :].rearrange("d f p -> d p f"))\
                       .then_inc(turn_read, 1)
                elif kind == "fold":
                    use = turn_use[step]
                    act.wait_ge(turned, use + 1)
                    act.copy(pairs[0:PAIR_PART, :, LAST * P:], turn_ps[0:PAIR_PART, use % 2, 0:PAIR_CHUNKS, :])\
                       .then_inc(turn_read, 1)
                elif kind == "onehot":
                    i = t
                    if i + 2 < PICKED:
                        split_hi(i + 2)
                    if i + 1 < PICKED:
                        last_block(i + 1)
                    use = acc_use[step]
                    act.wait_ge(acc_done, use + 1)
                    act.copy(vec[:, :, :, i], acc_ps[:, use % 2, :].rearrange("d (t p) -> d t p", t=TILES))\
                       .then_inc(acc_read, 1)
                elif kind == "gram":
                    use = gram_use[step]
                    if g == 0 and t >= 2:
                        act.wait_ge(dots_out, 32 * (t - 1))
                    act.wait_ge(gram_done, use + 1)
                    for s in (0, 1):
                        last = act.copy(dots_at(t, s, g), gram_read(s, use))
                    last.then_inc(gram_read_act, 1)
                elif kind == "square":
                    continue
                elif kind == "layer1":
                    use = acc_use[step]
                    if t == 0 and g == 0:
                        act.wait_ge(weights_in, 16 * WEIGHT_LOADS)
                    act.wait_ge(acc_done, use + 1)
                    act.activation(h1[:, g, :], acc_ps[:, use % 2, 0:P], ACT.Relu, bias=b1_sb[:, g:g + 1])\
                       .then_inc(acc_read, 1)
                elif kind == "layer2":
                    use = acc_use[step]
                    act.wait_ge(acc_done, use + 1)
                    act.activation(h2[:, t % 2, g, :], acc_ps[:, use % 2, 0:P], ACT.Relu, bias=b2_sb[:, g:g + 1])\
                       .then_inc(acc_read, 1)
                else:
                    use = acc_use[step]
                    act.wait_ge(acc_done, use + 1)
                    dst = y[:, :].rearrange("o (q s t) -> o s q t", s=QUAD, t=TILES)[:, :, :, t]
                    act.copy(dst, acc_ps[0:1, use % 2, 0:P].rearrange("o (s q) -> o s q", s=QUAD))\
                       .then_inc(acc_read, 1)

        @block.vector
        def _(dve):
            def make_hot(i, first, end):
                dve.wait_ge(pick_ids_in[i % IDS_SLOTS], 16 * (i // IDS_SLOTS + 1))
                for c in range(first, end):
                    if i >= 2:
                        dve.wait_ge(hot_used, (i - 2) * DVE_BLOCKS + c + 1)
                    dve.tensor_scalar(hot[:, (i * CHUNKS + c) % HOT_SLOTS, :], ids_rows[:, i % IDS_SLOTS, :],
                                      row_number[0:PICK_PART, c:c + 1], None, ALU.is_equal).then_inc(hot_made, 1)

            def split_lo(i):
                dve.wait_ge(table_in[i % 2], 32 * (i // 2 + 1))
                dve.wait_ge(hi_made, i + 1)
                if i >= SPLITS:
                    dve.wait_ge(acc_done, acc_use["onehot", i - SPLITS, 0] + 1)
                dve.tensor_tensor(table_lo[:, i % SPLITS, :], table[0:PICK_PART, i % 2, :],
                                  table_hi[:, i % SPLITS, :].bitcast(F32), ALU.subtract).then_inc(lo_made, 1)

            dve.memset(vec[:, :, :, FEATURES:], 0.0).then_inc(padded, 1)
            dve.wait_ge(rows_numbered, 1)
            dve.tensor_copy(row_number[:, :], row_number_i[:, :]).then_inc(numbers_float, 1)
            dve.tensor_scalar(minus_row[:, :], row_number_i[:, CHUNKS - 1:CHUNKS], -1.0, None, ALU.mult)\
               .then_inc(numbers_float, 1)
            dve.wait_ge(numbers_float, 1)
            make_hot(0, 0, FIRST_HOT)
            split_lo(0)
            make_hot(0, FIRST_HOT, DVE_BLOCKS)
            for step in order:
                kind, t, g = step
                if kind == "onehot":
                    if t + 1 < PICKED:
                        split_lo(t + 1)
                        make_hot(t + 1, 0, DVE_BLOCKS)
                elif kind == "gram":
                    use = gram_use[step]
                    if g == 0 and t >= 2:
                        dve.wait_ge(dots_out, 32 * (t - 1))
                    dve.wait_ge(gram_done, use + 1)
                    for s in (2, 3):
                        last = dve.tensor_copy(dots_at(t, s, g), gram_read(s, use))
                    last.then_inc(gram_read_dve, 1)
                elif kind == "square":
                    dve.wait_ge(square_done, g + 1)
                    n0, n1 = (0, SQUARE_M - STEPS) if g == 0 else (SQUARE_M - STEPS, FEATURES)
                    first = square_ps[:, 32 + 33 * n0:]
                    src = bass.AP(first.tensor, first.offset, [first.ap[0], [33, n1 - n0], [32, STEPS]])
                    dve.tensor_copy(z[:, :].rearrange("p (n k) -> p n k", k=STEPS)[:, n0:n1, :], src).then_inc(z_made, 1)


def pair_rows():
    dense_row = FEATURES * (FEATURES - 1) // 2
    rows = []
    for c in range(PAIR_CHUNKS):
        for n in range(c * PAIR_N, (c + 1) * PAIR_N):
            for k in range(1, STEPS + 1):
                i, j = sorted((SLOT_FEATURE[n], SLOT_FEATURE[(n + k) % FEATURES]))
                rows.append(j * (j - 1) // 2 + i)
        extra = K_ROWS[c] - PAIR_PART
        rows += range(dense_row, dense_row + extra)
        dense_row += extra
    return rows


def kernel(**inputs):
    import numpy as np
    import concourse.bacc as bacc
    from concourse.bass_utils import run_bass_kernel_spmd

    arrays = {"ids": inputs["ids"]}
    for f in range(FEATURES):
        arrays[f"tbl_{f}"] = inputs[f"tbl_{f}"]
    arrays["pick_ids"] = np.asarray(inputs["ids"])[:, PICK_FEATURES].reshape(P, TILES, PICKED).transpose(2, 1, 0)\
        .reshape(PICKED, BATCH)
    arrays["dense"] = np.asarray(inputs["dense_ctx"]).reshape(QUADS, QUAD, TILES, DENSE).transpose(3, 2, 1, 0)\
        .reshape(DENSE, BATCH)
    arrays["w1"] = np.asarray(inputs["W_top1"])[np.array(pair_rows())]
    arrays["b1"] = np.asarray(inputs["b_top1"]).reshape(OUT1, P).T
    arrays["w2"] = inputs["W_top2"]
    arrays["b2"] = np.asarray(inputs["b_top2"]).reshape(OUT2, P).T
    arrays["w3"] = np.asarray(inputs["W_top3"]).reshape(OUT2, P).T

    nc = bacc.Bacc("TRN2", target_bir_lowering=False, num_devices=1)
    feeds, aps = {}, {}
    for name, a in arrays.items():
        a = np.ascontiguousarray(a)
        feeds[f"in_{name}"] = a
        aps[name] = nc.dram_tensor(f"in_{name}", a.shape, mybir.dt.from_np(a.dtype), kind="ExternalInput").ap()
    out = nc.dram_tensor("out_y", (BATCH, 1), F32, kind="ExternalOutput").ap()
    build(nc, aps["ids"], aps["pick_ids"], aps["dense"], [aps[f"tbl_{f}"] for f in range(FEATURES)], aps["w1"], aps["b1"],
          aps["w2"], aps["b2"], aps["w3"], out)
    result = run_bass_kernel_spmd(nc, [feeds], core_ids=[0])
    return result.results[0]["out_y"]
```
